# Optimizing a Trainium2 kernel written in Bass

```python
import numpy as np
import jax
import jax.numpy as jnp

def _softmax(x, axis=-1):
    return jax.nn.softmax(x, axis=axis)

def _gelu(x):
    return jax.nn.gelu(x, approximate=True)

def _silu(x):
    return jax.nn.silu(x)

def _sigmoid(x):
    return jax.nn.sigmoid(x)

def _layernorm(x, axis=-1, eps=1e-05):
    m = jnp.mean(x, axis=axis, keepdims=True)
    v = jnp.var(x, axis=axis, keepdims=True)
    return (x - m) / jnp.sqrt(v + eps)

def _scatter_add(tgt, idx, src, axis=0):
    return tgt.at[idx].add(src)

def _segment_sum(src, seg, n):
    return jax.ops.segment_sum(src, seg, n)
kernel_name = 'mk_dlrm_tower_d1_rec_r8_016a29'

def setup_inputs(seed: int=0):
    np.random.seed(seed)
    _w = jnp.asarray

    def _rec_inputs():
        import jax
        import jax.numpy as jnp
        _tk = jax.random.key(seed)
        dense_ctx = jax.random.normal(jax.random.fold_in(_tk, 190), (512, 16), jnp.float32)
        ids = jnp.stack([jax.random.randint(jax.random.fold_in(_tk, 200 + f), (512,), 0, v, jnp.int32) for f, v in enumerate([1000, 1250, 1000, 125000, 1250, 1250, 125000, 125000, 12500, 12500, 1000, 1250, 12500, 12500, 1250, 1250, 125000, 1250, 1000, 1000, 12500, 1250, 125000, 1250, 1250, 1250, 1000, 125000, 1250, 125000, 1250, 125000])], axis=1)
        tbl_0 = 0.05 * jax.random.normal(jax.random.fold_in(_tk, 500 + 0), (1000, 16), jnp.float32)
        tbl_1 = 0.05 * jax.random.normal(jax.random.fold_in(_tk, 500 + 1), (1250, 16), jnp.float32)
        tbl_2 = 0.05 * jax.random.normal(jax.random.fold_in(_tk, 500 + 2), (1000, 16), jnp.float32)
        tbl_3 = 0.05 * jax.random.normal(jax.random.fold_in(_tk, 500 + 3), (125000, 16), jnp.float32)
        tbl_4 = 0.05 * jax.random.normal(jax.random.fold_in(_tk, 500 + 4), (1250, 16), jnp.float32)
        tbl_5 = 0.05 * jax.random.normal(jax.random.fold_in(_tk, 500 + 5), (1250, 16), jnp.float32)
        tbl_6 = 0.05 * jax.random.normal(jax.random.fold_in(_tk, 500 + 6), (125000, 16), jnp.float32)
        tbl_7 = 0.05 * jax.random.normal(jax.random.fold_in(_tk, 500 + 7), (125000, 16), jnp.float32)
        tbl_8 = 0.05 * jax.random.normal(jax.random.fold_in(_tk, 500 + 8), (12500, 16), jnp.float32)
        tbl_9 = 0.05 * jax.random.normal(jax.random.fold_in(_tk, 500 + 9), (12500, 16), jnp.float32)
        tbl_10 = 0.05 * jax.random.normal(jax.random.fold_in(_tk, 500 + 10), (1000, 16), jnp.float32)
        tbl_11 = 0.05 * jax.random.normal(jax.random.fold_in(_tk, 500 + 11), (1250, 16), jnp.float32)
        tbl_12 = 0.05 * jax.random.normal(jax.random.fold_in(_tk, 500 + 12), (12500, 16), jnp.float32)
        tbl_13 = 0.05 * jax.random.normal(jax.random.fold_in(_tk, 500 + 13), (12500, 16), jnp.float32)
        tbl_14 = 0.05 * jax.random.normal(jax.random.fold_in(_tk, 500 + 14), (1250, 16), jnp.float32)
        tbl_15 = 0.05 * jax.random.normal(jax.random.fold_in(_tk, 500 + 15), (1250, 16), jnp.float32)
        tbl_16 = 0.05 * jax.random.normal(jax.random.fold_in(_tk, 500 + 16), (125000, 16), jnp.float32)
        tbl_17 = 0.05 * jax.random.normal(jax.random.fold_in(_tk, 500 + 17), (1250, 16), jnp.float32)
        tbl_18 = 0.05 * jax.random.normal(jax.random.fold_in(_tk, 500 + 18), (1000, 16), jnp.float32)
        tbl_19 = 0.05 * jax.random.normal(jax.random.fold_in(_tk, 500 + 19), (1000, 16), jnp.float32)
        tbl_20 = 0.05 * jax.random.normal(jax.random.fold_in(_tk, 500 + 20), (12500, 16), jnp.float32)
        tbl_21 = 0.05 * jax.random.normal(jax.random.fold_in(_tk, 500 + 21), (1250, 16), jnp.float32)
        tbl_22 = 0.05 * jax.random.normal(jax.random.fold_in(_tk, 500 + 22), (125000, 16), jnp.float32)
        tbl_23 = 0.05 * jax.random.normal(jax.random.fold_in(_tk, 500 + 23), (1250, 16), jnp.float32)
        tbl_24 = 0.05 * jax.random.normal(jax.random.fold_in(_tk, 500 + 24), (1250, 16), jnp.float32)
        tbl_25 = 0.05 * jax.random.normal(jax.random.fold_in(_tk, 500 + 25), (1250, 16), jnp.float32)
        tbl_26 = 0.05 * jax.random.normal(jax.random.fold_in(_tk, 500 + 26), (1000, 16), jnp.float32)
        tbl_27 = 0.05 * jax.random.normal(jax.random.fold_in(_tk, 500 + 27), (125000, 16), jnp.float32)
        tbl_28 = 0.05 * jax.random.normal(jax.random.fold_in(_tk, 500 + 28), (1250, 16), jnp.float32)
        tbl_29 = 0.05 * jax.random.normal(jax.random.fold_in(_tk, 500 + 29), (125000, 16), jnp.float32)
        tbl_30 = 0.05 * jax.random.normal(jax.random.fold_in(_tk, 500 + 30), (1250, 16), jnp.float32)
        tbl_31 = 0.05 * jax.random.normal(jax.random.fold_in(_tk, 500 + 31), (125000, 16), jnp.float32)
        _rk = jax.random.fold_in(_tk, 7)
        W_top1 = 0.0693375 * jax.random.normal(jax.random.fold_in(_tk, 801), (208, 512), jnp.float32)
        W_top2 = 0.0441942 * jax.random.normal(jax.random.fold_in(_tk, 802), (512, 256), jnp.float32)
        W_top3 = 0.0625 * jax.random.normal(jax.random.fold_in(_tk, 803), (256, 1), jnp.float32)
        b_top1 = jnp.zeros((512,), jnp.float32)
        b_top2 = jnp.zeros((256,), jnp.float32)
        return (dense_ctx, ids, tbl_0, tbl_1, tbl_2, tbl_3, tbl_4, tbl_5, tbl_6, tbl_7, tbl_8, tbl_9, tbl_10, tbl_11, tbl_12, tbl_13, tbl_14, tbl_15, tbl_16, tbl_17, tbl_18, tbl_19, tbl_20, tbl_21, tbl_22, tbl_23, tbl_24, tbl_25, tbl_26, tbl_27, tbl_28, tbl_29, tbl_30, tbl_31, W_top1, b_top1, W_top2, b_top2, W_top3)
    dense_ctx, ids, tbl_0, tbl_1, tbl_2, tbl_3, tbl_4, tbl_5, tbl_6, tbl_7, tbl_8, tbl_9, tbl_10, tbl_11, tbl_12, tbl_13, tbl_14, tbl_15, tbl_16, tbl_17, tbl_18, tbl_19, tbl_20, tbl_21, tbl_22, tbl_23, tbl_24, tbl_25, tbl_26, tbl_27, tbl_28, tbl_29, tbl_30, tbl_31, W_top1, b_top1, W_top2, b_top2, W_top3 = _rec_inputs()

    def _L0_rec_setup():
        import jax, jax.numpy as jnp
        import numpy as np
        B, M, D = (2048, 32, 16)
        LAYERS = [64, 64, 64]
        key = jax.random.key(seed)
        ks = jax.random.split(key, 4)
        inp = {'embeddings': jax.random.normal(ks[0], (B, M, D), dtype=jnp.float32)}
        hk_1 = M
        for i, hk in enumerate(LAYERS):
            scale = (2.0 / (M * hk_1 + hk)) ** 0.5
            inp[f'W{i}'] = jax.random.normal(ks[i + 1], (M, hk_1, hk), dtype=jnp.float32) * scale
            hk_1 = hk
        return inp
    _L0_rec_all = _L0_rec_setup()
    _L0_rec_in = {k: v for k, v in _L0_rec_all.items() if k in ('W0', 'W1', 'W2')}
    del _L0_rec_all
    return {'dense_ctx': dense_ctx, 'ids': ids, 'tbl_0': tbl_0, 'tbl_1': tbl_1, 'tbl_2': tbl_2, 'tbl_3': tbl_3, 'tbl_4': tbl_4, 'tbl_5': tbl_5, 'tbl_6': tbl_6, 'tbl_7': tbl_7, 'tbl_8': tbl_8, 'tbl_9': tbl_9, 'tbl_10': tbl_10, 'tbl_11': tbl_11, 'tbl_12': tbl_12, 'tbl_13': tbl_13, 'tbl_14': tbl_14, 'tbl_15': tbl_15, 'tbl_16': tbl_16, 'tbl_17': tbl_17, 'tbl_18': tbl_18, 'tbl_19': tbl_19, 'tbl_20': tbl_20, 'tbl_21': tbl_21, 'tbl_22': tbl_22, 'tbl_23': tbl_23, 'tbl_24': tbl_24, 'tbl_25': tbl_25, 'tbl_26': tbl_26, 'tbl_27': tbl_27, 'tbl_28': tbl_28, 'tbl_29': tbl_29, 'tbl_30': tbl_30, 'tbl_31': tbl_31, 'W_top1': W_top1, 'b_top1': b_top1, 'W_top2': W_top2, 'b_top2': b_top2, 'W_top3': W_top3, 'L0_rec_W0': _L0_rec_in['W0'], 'L0_rec_W1': _L0_rec_in['W1'], 'L0_rec_W2': _L0_rec_in['W2']}

def reference(dense_ctx, ids, tbl_0, tbl_1, tbl_2, tbl_3, tbl_4, tbl_5, tbl_6, tbl_7, tbl_8, tbl_9, tbl_10, tbl_11, tbl_12, tbl_13, tbl_14, tbl_15, tbl_16, tbl_17, tbl_18, tbl_19, tbl_20, tbl_21, tbl_22, tbl_23, tbl_24, tbl_25, tbl_26, tbl_27, tbl_28, tbl_29, tbl_30, tbl_31, W_top1, b_top1, W_top2, b_top2, W_top3, L0_rec_W0, L0_rec_W1, L0_rec_W2):
    import jax
    import jax.numpy as jnp

    def _L0_rec_ref(embeddings, W0, W1, W2):
        import jax, jax.numpy as jnp
        import numpy as np
        B, M, D = (2048, 32, 16)
        LAYERS = [64, 64, 64]
        x0 = embeddings
        xk = x0
        outs = []
        for W in (W0, W1, W2):
            xk = jax.nn.relu(jnp.einsum('bmd,bhd,mhk->bkd', x0, xk, W))
            outs.append(jnp.sum(xk, axis=2))
        return jnp.concatenate(outs, axis=1)
    e = jnp.stack([tbl_0[ids[:, 0]], tbl_1[ids[:, 1]], tbl_2[ids[:, 2]], tbl_3[ids[:, 3]], tbl_4[ids[:, 4]], tbl_5[ids[:, 5]], tbl_6[ids[:, 6]], tbl_7[ids[:, 7]], tbl_8[ids[:, 8]], tbl_9[ids[:, 9]], tbl_10[ids[:, 10]], tbl_11[ids[:, 11]], tbl_12[ids[:, 12]], tbl_13[ids[:, 13]], tbl_14[ids[:, 14]], tbl_15[ids[:, 15]], tbl_16[ids[:, 16]], tbl_17[ids[:, 17]], tbl_18[ids[:, 18]], tbl_19[ids[:, 19]], tbl_20[ids[:, 20]], tbl_21[ids[:, 21]], tbl_22[ids[:, 22]], tbl_23[ids[:, 23]], tbl_24[ids[:, 24]], tbl_25[ids[:, 25]], tbl_26[ids[:, 26]], tbl_27[ids[:, 27]], tbl_28[ids[:, 28]], tbl_29[ids[:, 29]], tbl_30[ids[:, 30]], tbl_31[ids[:, 31]]], axis=1)
    z = _L0_rec_ref(e, L0_rec_W0, L0_rec_W1, L0_rec_W2)
    z = z.reshape(z.shape[0], -1)
    h = jnp.concatenate([z, dense_ctx], axis=1)
    h = jnp.maximum(h @ W_top1 + b_top1, 0.0)
    h = jnp.maximum(h @ W_top2 + b_top2, 0.0)
    y = h @ W_top3
    return y

_drawn_inputs = setup_inputs


def setup_inputs(seed=0):
    import zlib

    import numpy as np

    out = dict(_drawn_inputs(seed))
    spreads = {'b_top1': (0.0, 2.0), 'b_top2': (0.0, 0.8)}
    factors = {'tbl_0': 8.0,
     'tbl_1': 8.0,
     'tbl_2': 8.0,
     'tbl_3': 8.0,
     'tbl_4': 8.0,
     'tbl_5': 8.0,
     'tbl_6': 8.0,
     'tbl_7': 8.0,
     'tbl_8': 8.0,
     'tbl_9': 8.0,
     'tbl_10': 8.0,
     'tbl_11': 8.0,
     'tbl_12': 8.0,
     'tbl_13': 8.0,
     'tbl_14': 8.0,
     'tbl_15': 8.0,
     'tbl_16': 8.0,
     'tbl_17': 8.0,
     'tbl_18': 8.0,
     'tbl_19': 8.0,
     'tbl_20': 8.0,
     'tbl_21': 8.0,
     'tbl_22': 8.0,
     'tbl_23': 8.0,
     'tbl_24': 8.0,
     'tbl_25': 8.0,
     'tbl_26': 8.0,
     'tbl_27': 8.0,
     'tbl_28': 8.0,
     'tbl_29': 8.0,
     'tbl_30': 8.0,
     'tbl_31': 8.0,
     'L0_rec_W0': 3.544,
     'L0_rec_W1': 8.0,
     'L0_rec_W2': 8.0,
     'dense_ctx': 7.091}
    for name, (base, spread) in spreads.items():
        noise = np.random.default_rng([zlib.crc32(name.encode()), seed]).standard_normal(out[name].shape)
        drawn = base * np.exp(spread * noise) if base else spread * noise
        out[name] = jnp.asarray(drawn.astype(out[name].dtype))
    for name, factor in factors.items():
        out[name] = (out[name] * factor).astype(out[name].dtype)
    return out
```

```python
from contextlib import ExitStack

import concourse.bass as bass
from concourse import mybir

F32 = mybir.dt.float32
BF16 = mybir.dt.bfloat16
I32 = mybir.dt.int32
ALU = mybir.AluOpType
ACT = mybir.ActivationFunctionType
AX_X = mybir.AxisListType.X

B, F, D, K = 512, 32, 16, 64
P = 128
BLOCKS = B // P
PARTS = 4
PW = P * D // PARTS
HALF = PW // 2
DP = D // PARTS
TILES = F * K // P
TILES0 = 5
NCTX = 16
N1, N2 = 512, 256

PE_TILES = 8
UNITS = PE_TILES // 2
ZSLOTS = 4
LAG = 2
SLOT = [0, 1, 2, 0]
STEPS = [(1, 0), (1, 1), (2, 0), (1, 2), (2, 1), (1, 3), (2, 2), (2, 3)]
POOL_MULS = {(1, 1, 3), (1, 2, 3), (1, 3, 3), (2, 3, 1)}


def tiles_of(layer, g):
    return range(2 * g, min(2 * g + 2, TILES0)) if layer == 0 else range(4 * g, 4 * g + 4)


def groups(layer):
    return 3 if layer == 0 else 4


class Lagged:

    def __init__(self):
        self.events, self.waiting = [], []

    def add(self, *events):
        self.events += events

    def product(self, layer, part, g):
        self.add(("mul", layer, part, g))
        self.waiting.append((layer, part, g))
        if len(self.waiting) > LAG:
            self.matmuls()

    def matmuls(self):
        layer, part, g = self.waiting.pop(0)
        self.add(("mm", layer, part, g))
        if g == groups(layer) - 1:
            self.add(("relu", layer, part))
            if part > 0:
                self.add(("sum", layer, part))

    def drain(self):
        while self.waiting:
            self.matmuls()


def layer0(order, mlp):
    order.add(("load", 0))
    for n in range(PARTS * 3):
        part, g = divmod(n, 3)
        order.add(("rot", part, g))
        order.product(0, part, g)
        if n < 4:
            order.add(*[("wide", 0, u) for u in range(n, UNITS, 4)])
        elif 6 <= n < 10:
            order.add(*[("wide", 2, u) for u in range(n - 6, UNITS, 4)])
        if mlp and n == 4:
            order.add(("fold", 2))
        if mlp and n in (5, 8, 10):
            order.add(("mlp", {5: 1, 8: 2, 10: 3}[n]))
    order.drain()


def prologue():
    order = Lagged()
    order.add(("ids",), *[("gather", f) for f in range(F)], ("spread",))
    order.add(("turn", 0), ("park", 0), ("turn", 1), ("park", 1), ("split", 0), ("turn", 2), ("park", 2),
              ("split", 1), ("turn", 3), ("park", 3), ("split", 2), ("split", 3))
    order.add(("load", 1), ("load", 2), *[("wide", 1, u) for u in range(UNITS)])
    layer0(order, False)
    return order.events


def block_order(last):
    order = Lagged()
    extra = {}

    def at(step, g, *events):
        extra.setdefault((step, g), []).extend(events)

    at(3, 0, ("load", 3))
    for u in range(UNITS):
        at(3 + u // 4, u % 4, ("wide", 3, u))
    at(7, 2, ("fold", 1))
    if not last:
        at(0, 0, ("ids",))
        for f in range(F):
            n = f * 20 // F
            at(n // 4, n % 4, ("gather", f))
        at(5, 1, ("spread",))
        at(5, 2, ("turn", 0), ("park", 0))
        at(5, 3, ("turn", 1), ("park", 1))
        at(6, 0, ("split", 0))
        at(6, 1, ("turn", 2), ("park", 2))
        at(6, 2, ("split", 1), ("turn", 3), ("park", 3))
        at(6, 3, ("split", 2), ("load", 1))
        at(7, 0, ("split", 3), ("load", 2))
        for u in range(UNITS):
            at(7, u % 4, ("wide", 1, u))
    for step, (layer, part) in enumerate(STEPS):
        for g in range(4):
            order.product(layer, part, g)
            order.add(*extra.get((step, g), []))
    if last:
        order.drain()
        order.add(("fold", 2), ("mlp", 1), ("mlp", 2), ("mlp", 3))
    else:
        layer0(order, True)
    return order.events


PROLOGUE, BODY, LAST = prologue(), block_order(False), block_order(True)


class Phase:

    def __init__(self, events, i):
        self.events, self.i = events, i
        self.next = 0 if i is None else i + 1


class Tally:

    def __init__(self, adds):
        self.adds = adds
        self.first, self.turn = (sum(map(adds, e)) for e in (PROLOGUE, BODY))

    def base(self, phase):
        return 0 if phase.i is None else phase.i * self.turn + self.first

    def after(self, phase, event, extra=0):
        local = sum(map(self.adds, phase.events[:phase.events.index(event) + 1]))
        return self.base(phase) + (local + extra)

    def back(self, phase, event, steps):
        value = self.after(phase, event, -steps)
        if phase.i is None and value < 1:
            return None
        return value

    def before(self, phase):
        return self.base(phase)


def is_kind(*kinds):
    return lambda e: int(e[0] in kinds)


dve_muls = Tally(lambda e: int(e[0] == "mul" and e[1:] not in POOL_MULS))
pool_muls = Tally(lambda e: int(e[0] == "mul" and e[1:] in POOL_MULS))
products = Tally(is_kind("mul"))
consumed = Tally(is_kind("mm"))
steps_done = Tally(is_kind("relu"))
relus = Tally(lambda e: 0 if e[0] != "relu" else 8 if e[1] < 2 and e[2] == 0 else 4)
sums = Tally(is_kind("sum"))
units = Tally(is_kind("wide", "rot"))
wides = Tally(is_kind("wide"))
turns = Tally(is_kind("turn"))
x0s = Tally(lambda e: 3 * int(e[0] == "turn"))
splits = Tally(lambda e: int(e[0] in ("turn", "split")))
mids = Tally(is_kind("split"))
spreads = Tally(is_kind("spread"))
gathers = Tally(lambda e: 16 * int(e[0] == "gather"))
idloads = Tally(lambda e: 16 * int(e[0] == "ids"))
folds = Tally(lambda e: {1: 2, 2: 1}[e[1]] if e[0] == "fold" else 0)
mlps = Tally(is_kind("mlp"))
mlp_acts = Tally(lambda e: {1: 4, 2: 2, 3: 1}[e[1]] if e[0] == "mlp" else 0)


def unit_before(phase, event, back):
    at = phase.events.index(event)
    own = [e for e in phase.events[:at] if e[0] in ("wide", "rot")]
    if len(own) >= back:
        return own[-back], True
    if phase.i is None:
        return None
    tail = [e for e in PROLOGUE if e[0] in ("wide", "rot")]
    return tail[len(own) - back], False


def z_slot(phase, group):
    return [e for e in phase.events if e[0] == "mul"].index(("mul",) + group) % ZSLOTS


def unit_buffer(phase, event):
    return [e for e in phase.events if e[0] in ("wide", "rot")].index(event) % 2


def y_bank(phase, layer, part):
    return [e for e in phase.events if e[0] == "relu"].index(("relu", layer, part)) % 2


for _order in (PROLOGUE, BODY):
    assert sum(e[0] == "mul" for e in _order) % ZSLOTS == 0
    assert sum(e[0] in ("wide", "rot") for e in _order) % 2 == 0
    assert sum(e[0] == "relu" for e in _order) % 2 == 0


def build(nc, ins, out):
    tables = [ins[f"tbl_{f}"] for f in range(F)]
    x0_dram = nc.dram_tensor("x0_parked", (F, P * D), F32, kind="Internal").ap()

    with ExitStack() as ctx:
        def sb(name, shape, dt=F32):
            return ctx.enter_context(nc.sbuf_tensor(name, shape, dt))

        def ps(name, shape):
            return ctx.enter_context(nc.psum_tensor(name, shape, F32))

        def sem(name):
            return ctx.enter_context(nc.semaphore(name))

        idx = sb("idx", [P, F], I32)
        ids_seen = sb("ids_seen", [P, 2], I32)
        gathered = sb("gathered", [P, F * D])
        spread = sb("spread", [P, D, 4, F])
        x0 = sb("x0", [P, P * D])
        x0_split = sb("x0_split", [P, P * D], BF16)
        rest = sb("rest", [P, 2, PW])
        high = sb("high", [P, 2, PW], BF16)
        mid = sb("mid", [P, 2, PW], BF16)
        wide = [sb(f"wide{s}", [P, TILES, PW]) for s in range(3)]
        z = sb("z", [P, ZSLOTS, 4, PW])
        xk = sb("xk", [P, PARTS, PW])
        xlast = sb("xlast", [P, 2, PW])
        acc = [sb(f"acc{layer}", [P, PW]) for layer in range(3)]
        pooled01 = sb("pooled01", [P, P])
        pooled2 = sb("pooled2", [P, P])
        context = sb("context", [P, B])
        w0 = sb("w0", [P, TILES0, K])
        w0_mirror = sb("w0_mirror", [P, TILES0, K])
        w12 = sb("w12", [P, 2, TILES, K])
        top1a = sb("top1a", [P, N1])
        top1b = sb("top1b", [P, N1])
        top2 = sb("top2", [P, N1 // P, N2])
        top3 = sb("top3", [P, N2 // P])
        bias1 = sb("bias1", [P, N1 // P])
        bias2 = sb("bias2", [P, N2 // P])
        hid1 = sb("hid1", [P, N1 // P, P])
        hid2 = sb("hid2", [P, N2 // P, P])
        y_row = sb("y_row", [P, B])
        select = sb("select", [P, max(PE_TILES, 1), P], BF16)
        rotate = sb("rotate", [P, TILES0, P], BF16)
        ident = sb("ident", [P, P])

        ps_wide = ps("ps_wide", [P, 2, 2, PW])
        ps_y = ps("ps_y", [P, 2, 512])
        ps_turn = ps("ps_turn", [P, PW])
        ps_mlp = ps("ps_mlp", [P, 512])

        consts_in = sem("consts_in")
        w0_in = sem("w0_in")
        w12_in = sem("w12_in")
        top_in = sem("top_in")
        w0_ready = sem("w0_ready")
        ids_in = sem("ids_in")
        seen_zeroed = sem("seen_zeroed")
        zeroed = sem("zeroed")
        rows_in = sem("rows_in")
        spread_ready = sem("spread_ready")
        turned = sem("turned")
        x0_ready = sem("x0_ready")
        rest_ready = sem("rest_ready")
        mid_ready = sem("mid_ready")
        parked = [sem(f"parked{p}") for p in range(PARTS)]
        wide_in = [[sem(f"wide_in{s}_{g}") for g in range(4)] for s in range(3)]
        unit_ready = sem("unit_ready")
        wide_ready = sem("wide_ready")
        z_vector = sem("z_vector")
        z_pool = sem("z_pool")
        z_used = sem("z_used")
        xk_ready = sem("xk_ready")
        sum_done = sem("sum_done")
        folded = sem("folded")
        context_ready = sem("context_ready")
        mlp_ready = sem("mlp_ready")
        hid_ready = sem("hid_ready")
        out_done = sem("out_done")

        block = ctx.enter_context(nc.Block())

        def cols(part):
            return slice(part * PW, (part + 1) * PW)

        def wait_product(eng, phase, group):
            event = ("mul",) + group
            if group in POOL_MULS:
                eng.wait_ge(z_pool, pool_muls.after(phase, event))
            else:
                eng.wait_ge(z_vector, dve_muls.after(phase, event))

        def wait_wide_free(eng, phase, part, g):
            if phase.i is None:
                return
            owner = {3: 0, 0: 3, 1: 1, 2: 2}[part]
            wait_product(eng, phase, (2, owner, g))

        def wait_slot_free(eng, phase, event):
            value = products.back(phase, event, ZSLOTS)
            if value is not None:
                eng.wait_ge(z_used, value)

        def wait_wide_ready(eng, phase, part, g):
            mine = part == 3
            tiles = tiles_of(1, g)
            if tiles[0] < PE_TILES:
                event = ("wide", part, (tiles[-1]) // 2)
                if mine:
                    eng.wait_ge(wide_ready, wides.after(phase, event))
                else:
                    eng.wait_ge(wide_ready, wides.before(phase) - tail_rest(wides, event))
            else:
                loads = Tally(lambda e: 32 * int(e[0] == "load" and SLOT[e[1]] == SLOT[part]))
                if mine:
                    eng.wait_ge(wide_in[SLOT[part]][g], loads.after(phase, ("load", part)))
                else:
                    eng.wait_ge(wide_in[SLOT[part]][g], loads.before(phase))

        def tail_rest(tally, event):
            rest_p = sum(map(tally.adds, PROLOGUE[PROLOGUE.index(event) + 1:]))
            rest_b = sum(map(tally.adds, BODY[BODY.index(event) + 1:]))
            assert rest_p == rest_b
            return rest_p

        def wait_xk(eng, phase, layer, part):
            if layer == 1:
                eng.wait_ge(xk_ready, relus.before(phase) - tail_rest(relus, ("relu", 0, part)))
            else:
                eng.wait_ge(xk_ready, relus.after(phase, ("relu", 1, part)))

        def multiply(engine, phase, layer, part, g):
            t = tiles_of(layer, g)
            return engine.tensor_tensor(
                z[:, z_slot(phase, (layer, part, g))],
                xk[:, part, :].unsqueeze(1).broadcast_to([P, 4, PW]),
                wide[SLOT[part]][:, t[0]:t[-1] + 1, :], ALU.mult)

        def phases(eng, run):
            run(Phase(PROLOGUE, None))
            with eng.Fori(0, BLOCKS - 1) as i:
                run(Phase(BODY, i))
            run(Phase(LAST, BLOCKS - 1))

        @block.sync
        def _(sp):
            sp.dma_start(idx[:], ins["ids"][0:P, :]).then_inc(ids_in, 16)
            sp.dma_start(ident[:], ins["ident"]).then_inc(consts_in, 16)
            sp.dma_start(select[0:96], ins["select"]).then_inc(consts_in, 16)
            sp.dma_start(rotate[0:96], ins["rotate"]).then_inc(consts_in, 16)
            sp.dma_start(w0[:], ins["w0_pairs"].rearrange("(t p) k -> p t k", p=P)).then_inc(w0_in, 16)
            sp.dma_start(w0_mirror[:], ins["w0_mirror"].rearrange("(t p) k -> p t k", p=P)).then_inc(w0_in, 16)
            for n in (1, 2):
                sp.dma_start(w12[:, n - 1], ins[f"L0_rec_W{n}"].rearrange("m h k -> (m h) k")
                             .rearrange("(t p) k -> p t k", p=P)).then_inc(w12_in, 16)
            top = ins["W_top1"]
            sp.dma_start(top1a[:], top[0:P, :]).then_inc(top_in, 16)
            sp.dma_start(top1b[0:K + NCTX], top[P:, :]).then_inc(top_in, 16)
            sp.dma_start(top2[:], ins["W_top2"].rearrange("(t p) n -> p t n", p=P)).then_inc(top_in, 16)
            sp.dma_start(top3[:], ins["top3"]).then_inc(top_in, 16)
            sp.dma_start(bias1[:], ins["bias1"]).then_inc(top_in, 16)
            sp.dma_start(bias2[:], ins["bias2"]).then_inc(top_in, 16)
            sp.dma_start(context[K:K + NCTX], ins["context"]).then_inc(top_in, 16)

            def run(phase):
                for event in phase.events:
                    if event[0] == "ids" and phase.i is not None:
                        sp.wait_ge(rows_in, gathers.before(phase))
                        sp.dma_start(idx[:], ins["ids"][bass.ds(phase.next * P, P), :]).then_inc(ids_in, 16)

            phases(sp, run)
            sp.wait_ge(hid_ready, 7 * BLOCKS)
            sp.dma_start(out.rearrange("b one -> one b"), y_row[0:1, :]).then_inc(out_done, 16)
            sp.wait_ge(out_done, 16)
            for part in range(PARTS):
                sp.wait_ge(parked[part], 16 * BLOCKS)

        @block.gpsimd
        def _(pool):
            nc.gpsimd.memset(ids_seen[:], 0).then_inc(seen_zeroed, 1)
            pool.wait_ge(seen_zeroed, 1)
            pool.wait_ge(zeroed, 2)

            def run(phase):
                for event in phase.events:
                    kind = event[0]
                    if kind == "gather":
                        f = event[1]
                        if f == 0:
                            pool.wait_ge(ids_in, idloads.after(phase, ("ids",)))
                            nc.gpsimd.tensor_tensor(ids_seen[:, 1:2], ids_seen[:, 0:1], ids_seen[:, 0:1], ALU.add)
                        nc.gpsimd.indirect_dma_start(
                            gathered[:, f * D:(f + 1) * D], None, tables[f],
                            bass.IndirectOffsetOnAxis(ap=idx[:, f:f + 1], axis=0)).then_inc(rows_in, 16)
                    elif kind == "turn":
                        part = event[1]
                        pool.wait_ge(x0_ready, x0s.after(phase, event))
                        if part > 1:
                            pool.wait_ge(rest_ready, splits.after(phase, ("split", part - 2)))
                        nc.gpsimd.tensor_tensor(rest[:, part % 2], x0[:, cols(part)], high[:, part % 2],
                                                ALU.subtract).then_inc(rest_ready, 1)
                    elif kind == "split":
                        part = event[1]
                        pool.wait_ge(mid_ready, mids.after(phase, event))
                        nc.gpsimd.tensor_tensor(x0_split[:, cols(part)], rest[:, part % 2],
                                                mid[:, part % 2], ALU.subtract).then_inc(rest_ready, 1)
                    elif kind == "sum":
                        _, layer, part = event
                        if part > 1:
                            pool.wait_ge(sum_done, sums.after(phase, ("sum", layer, part - 1)))
                        pool.wait_ge(xk_ready, relus.after(phase, ("relu", layer, part)))
                        src = xlast[:, part % 2] if layer == 2 else xk[:, part]
                        nc.gpsimd.tensor_tensor(acc[layer][:], acc[layer][:], src, ALU.add).then_inc(sum_done, 1)
                    elif kind == "mul" and event[1:] in POOL_MULS:
                        _, layer, part, g = event
                        wait_slot_free(pool, phase, event)
                        wait_xk(pool, phase, layer, part)
                        wait_wide_ready(pool, phase, part, g)
                        multiply(nc.gpsimd, phase, layer, part, g).then_inc(z_pool, 1)

            phases(pool, run)

        @block.vector
        def _(dve):
            nc.vector.memset(high[:], 0.0).then_inc(zeroed, 1)
            nc.vector.memset(mid[:], 0.0).then_inc(zeroed, 1)
            dve.wait_ge(w0_in, 32)
            nc.vector.tensor_tensor(w0[:], w0[:], w0_mirror[:], ALU.add).then_inc(w0_ready, 1)

            def run(phase):
                for event in phase.events:
                    kind = event[0]
                    if kind == "mul" and event[1:] not in POOL_MULS:
                        _, layer, part, g = event
                        wait_slot_free(dve, phase, event)
                        if layer:
                            wait_xk(dve, phase, layer, part)
                            wait_wide_ready(dve, phase, part, g)
                            multiply(nc.vector, phase, layer, part, g).then_inc(z_vector, 1)
                        else:
                            dve.wait_ge(unit_ready, units.after(phase, ("rot", part, g)))
                            n = len(tiles_of(0, g))
                            buf = unit_buffer(phase, ("rot", part, g))
                            nc.vector.tensor_tensor(
                                z[:, z_slot(phase, (layer, part, g)), 0:n],
                                x0[:, cols(part)].unsqueeze(1).broadcast_to([P, n, PW]),
                                ps_wide[:, buf, 0:n], ALU.mult).then_inc(z_vector, 1)
                    elif kind == "fold":
                        dve.wait_ge(sum_done, sums.after(phase, ("sum", event[1], PARTS - 1)))
                        for layer in [(), (0, 1), (2,)][event[1]]:
                            rows = slice(K, P) if layer == 1 else slice(0, K)
                            pooled = pooled2 if layer == 2 else pooled01
                            nc.vector.tensor_reduce(pooled[rows], acc[layer][rows].rearrange("p (d b) -> p b d", d=DP),
                                                    AX_X, ALU.add).then_inc(folded, 1)

            phases(dve, run)

        @block.scalar
        def _(act):
            act.wait_ge(zeroed, 2)

            def run(phase):
                for event in phase.events:
                    kind = event[0]
                    if kind == "spread":
                        act.wait_ge(rows_in, gathers.after(phase, ("gather", F - 1)))
                        nc.scalar.activation(
                            spread[:], gathered[:].rearrange("p (f d) -> p d f", d=D).unsqueeze(2)
                            .broadcast_to([P, D, 4, F]), ACT.Copy).then_inc(spread_ready, 1)
                    elif kind == "turn":
                        part = event[1]
                        act.wait_ge(turned, turns.after(phase, event))
                        if phase.i is not None:
                            act.wait_ge(parked[part], phase.next * 16)
                        nc.scalar.activation(x0[:, cols(part)], ps_turn[:], ACT.Copy).then_inc(x0_ready, 1)
                        for rows in (slice(32, 64), slice(64, P)):
                            nc.scalar.activation(high[rows, part % 2], ps_turn[rows],
                                                 ACT.Copy).then_inc(x0_ready, 1)
                    elif kind == "park":
                        part = event[1]
                        act.wait_ge(x0_ready, x0s.after(phase, ("turn", part)))
                        if phase.i is not None:
                            for g in range(PE_TILES // 4, 4):
                                wait_product(act, phase, (1, part, g))
                        act.dma_start(x0_dram[:, cols(part)], x0[0:F, cols(part)]).then_inc(parked[part], 16)
                    elif kind == "load":
                        part = event[1]
                        bt = phase.i if part == 3 else phase.next
                        landed = (bt + 1) * 16
                        for g in range(PE_TILES // 4, 4):
                            wait_wide_free(act, phase, part, g)
                            if g == PE_TILES // 4:
                                act.wait_ge(parked[part], landed)
                            for half in range(2):
                                src = x0_dram[:, cols(part)].rearrange(
                                    "(t two) c -> two t c", two=2)[half:half + 1, 4 * g:4 * g + 4, :]
                                act.dma_start(wide[SLOT[part]][K * half:K * half + K, 4 * g:4 * g + 4, :],
                                             src.broadcast_to([K, 4, PW])).then_inc(wide_in[SLOT[part]][g], 16)
                    elif kind == "split":
                        part = event[1]
                        act.wait_ge(rest_ready, splits.after(phase, ("turn", part)))
                        nc.scalar.activation(mid[64:96, part % 2], rest[64:96, part % 2],
                                             ACT.Copy).then_inc(mid_ready, 1)
                    elif kind == "wide":
                        _, part, u = event
                        act.wait_ge(unit_ready, units.after(phase, event))
                        wait_wide_free(act, phase, part, u // 2)
                        nc.scalar.activation(wide[SLOT[part]][:, 2 * u:2 * u + 2, :],
                                             ps_wide[:, unit_buffer(phase, event)], ACT.Copy).then_inc(wide_ready, 1)
                    elif kind == "relu":
                        _, layer, part = event
                        act.wait_ge(z_used, consumed.after(phase, ("mm", layer, part, groups(layer) - 1)))
                        bank = y_bank(phase, layer, part)
                        if layer == 2 and part > 2:
                            act.wait_ge(sum_done, sums.after(phase, ("sum", 2, part - 2)))
                        if layer == 1 and part > 0:
                            act.wait_ge(sum_done, sums.before(phase) - tail_rest(sums, ("sum", 0, part)))
                        if layer == 0 and phase.i is not None:
                            if part > 0:
                                act.wait_ge(sum_done, sums.after(phase, ("sum", 1, part)))
                            else:
                                act.wait_ge(folded, folds.after(phase, ("fold", 1)))
                        dsts = [xk[:, part] if layer < 2 else xlast[:, part % 2]]
                        if part == 0:
                            dsts = (dsts if layer < 2 else []) + [acc[layer]]
                        for dst in dsts:
                            for c in range(2):
                                for half in range(2):
                                    nc.scalar.activation(dst[K * half:K * half + K, c * HALF:(c + 1) * HALF],
                                                         ps_y[c * K:c * K + K, bank, 0:HALF],
                                                         ACT.Relu).then_inc(xk_ready, 1)
                    elif kind == "fold" and event[1] == 1:
                        act.wait_ge(top_in, 7 * 16)
                        nc.scalar.activation(pooled2[K:K + NCTX], context[K:K + NCTX, bass.ds(phase.i * P, P)],
                                             ACT.Copy).then_inc(context_ready, 1)
                    elif kind == "mlp":
                        n = event[1]
                        act.wait_ge(mlp_ready, mlps.after(phase, event))
                        if n == 3:
                            nc.scalar.activation(y_row[0:1, bass.ds(phase.i * P, P)], ps_mlp[0:1, 0:P],
                                                 ACT.Copy).then_inc(hid_ready, 1)
                        hid, bias, chunks = [(hid1, bias1, N1 // P), (hid2, bias2, N2 // P), (None, None, 0)][n - 1]
                        for q in range(chunks):
                            nc.scalar.activation(hid[:, q], ps_mlp[:, q * P:(q + 1) * P], ACT.Relu,
                                                 bias=bias[:, q:q + 1]).then_inc(hid_ready, 1)

            phases(act, run)

        @block.tensor
        def _(pe):
            pe.wait_ge(consts_in, 3 * 16)

            def run(phase):
                for event in phase.events:
                    kind = event[0]
                    if kind == "turn":
                        part = event[1]
                        if part == 0:
                            pe.wait_ge(spread_ready, spreads.after(phase, ("spread",)))
                        value = x0s.back(phase, event, 3)
                        if value is not None:
                            pe.wait_ge(x0_ready, value)
                        for j in range(DP):
                            mm = nc.tensor.transpose(
                                ps_turn[:, j * P:(j + 1) * P],
                                spread[:, part * DP + j].rearrange("p r f -> p (r f)"), ident[:])
                        mm.then_inc(turned, 1)
                    elif kind in ("wide", "rot"):
                        _, part, u = event
                        before = unit_before(phase, event, 2)
                        if before is not None:
                            (k2, p2, u2), own = before
                            if k2 == "wide":
                                s, tally, e2 = wide_ready, wides, before[0]
                            else:
                                s, tally, e2 = z_vector, dve_muls, ("mul", 0, p2, u2)
                            pe.wait_ge(s, tally.after(phase, e2) if own
                                       else tally.before(phase) - tail_rest(tally, e2))
                        if kind == "rot" or part != 3:
                            pe.wait_ge(rest_ready, splits.after(phase, ("split", part)))
                        buf = unit_buffer(phase, event)
                        table, tiles = (select, range(2 * u, 2 * u + 2)) if kind == "wide" else (rotate, tiles_of(0, u))
                        for n, t in enumerate(tiles):
                            mm = nc.tensor.matmul(ps_wide[:, buf, n], table[0:96, t], x0_split[0:96, cols(part)],
                                                  start=True, stop=True)
                        mm.then_inc(unit_ready, 1)
                    elif kind == "mm":
                        _, layer, part, g = event
                        wait_product(pe, phase, event[1:])
                        if g == 0:
                            order = [e for e in phase.events if e[0] == "relu"]
                            n = order.index(("relu", layer, part))
                            if n >= 2:
                                pe.wait_ge(xk_ready, relus.after(phase, order[n - 2]))
                            elif phase.i is not None:
                                pe.wait_ge(xk_ready, relus.before(phase) - tail_rest(relus, ("relu", 0, 2 + n)))
                            if phase.i is None and part == 0:
                                pe.wait_ge(w0_ready, 1)
                            if layer == 1 and part == 0:
                                pe.wait_ge(w12_in, 32)
                        bank, slot = y_bank(phase, layer, part), z_slot(phase, (layer, part, g))
                        total = TILES if layer else TILES0
                        for n, t in enumerate(tiles_of(layer, g)):
                            weights = w12[:, layer - 1, t] if layer else w0[:, t]
                            for c in range(2):
                                mm = nc.tensor.matmul(ps_y[K * c:K * c + K, bank, 0:HALF], weights,
                                                      z[:, slot, n, c * HALF:(c + 1) * HALF],
                                                      start=t == 0, stop=t == total - 1)
                        mm.then_inc(z_used, 1)
                    elif kind == "mlp" and event[1] == 1:
                        pe.wait_ge(folded, folds.after(phase, ("fold", 2)))
                        pe.wait_ge(context_ready, folds_of_context.after(phase, ("fold", 1)))
                        for q in range(N1 // P):
                            nc.tensor.matmul(ps_mlp[:, q * P:(q + 1) * P], top1a[:, q * P:(q + 1) * P],
                                             pooled01[:], start=True, stop=False)
                            mm = nc.tensor.matmul(ps_mlp[:, q * P:(q + 1) * P], top1b[0:K + NCTX, q * P:(q + 1) * P],
                                                  pooled2[0:K + NCTX], start=False, stop=True)
                        mm.then_inc(mlp_ready, 1)
                    elif kind == "mlp" and event[1] == 2:
                        pe.wait_ge(hid_ready, mlp_acts.after(phase, ("mlp", 1)))
                        for q in range(N2 // P):
                            for t in range(N1 // P):
                                mm = nc.tensor.matmul(ps_mlp[:, q * P:(q + 1) * P], top2[:, t, q * P:(q + 1) * P],
                                                      hid1[:, t], start=t == 0, stop=t == N1 // P - 1)
                        mm.then_inc(mlp_ready, 1)
                    elif kind == "mlp":
                        pe.wait_ge(hid_ready, mlp_acts.after(phase, ("mlp", 2)))
                        for t in range(N2 // P):
                            mm = nc.tensor.matmul(ps_mlp[0:1, 0:P], top3[:, t:t + 1], hid2[:, t],
                                                  start=t == 0, stop=t == N2 // P - 1)
                        mm.then_inc(mlp_ready, 1)

            phases(pe, run)


folds_of_context = Tally(lambda e: int(e == ("fold", 1)))


def kernel(**inputs):
    import ml_dtypes
    import numpy as np
    from concourse import bacc
    from concourse.bass_utils import run_bass_kernel_spmd

    w = np.asarray(inputs["L0_rec_W0"])
    h = np.arange(F)
    pairs = np.zeros((4 * TILES0, F, K), w.dtype)
    mirror = np.zeros((4 * TILES0, F, K), w.dtype)
    for j in range(F // 2 + 1):
        pairs[j] = w[h, (h + j) % F]
        if 0 < j < F // 2:
            mirror[j] = w[(h + j) % F, h]

    select = np.zeros((3, F, max(PE_TILES, 1), P), np.float32)
    rotate = np.zeros((3, F, TILES0, P), np.float32)
    for t in range(PE_TILES):
        for p in range(P):
            select[:, 2 * t + p // K, t, p] = 1
    for j in range(F // 2 + 1):
        for m in range(F):
            rotate[:, (m + j) % F, j // 4, j % 4 * F + m] = 1

    arrays = {k: np.ascontiguousarray(inputs[k]) for k in
              ["ids"] + [f"tbl_{f}" for f in range(F)]
              + ["W_top1", "W_top2", "L0_rec_W1", "L0_rec_W2"]}
    for name, key in (("bias1", "b_top1"), ("bias2", "b_top2"), ("top3", "W_top3")):
        arrays[name] = np.ascontiguousarray(np.asarray(inputs[key]).reshape(-1, P).T)
    arrays["context"] = np.ascontiguousarray(np.asarray(inputs["dense_ctx"]).T)
    arrays["w0_pairs"] = pairs.reshape(-1, K)
    arrays["w0_mirror"] = mirror.reshape(-1, K)
    arrays["select"] = select.reshape(3 * F, -1, P).astype(ml_dtypes.bfloat16)
    arrays["rotate"] = rotate.reshape(3 * F, -1, P).astype(ml_dtypes.bfloat16)
    arrays["ident"] = np.eye(P, dtype=np.float32)

    nc = bacc.Bacc("TRN2", target_bir_lowering=False, num_devices=1)
    ins = {name: nc.dram_tensor(f"in_{name}_dram", a.shape, mybir.dt.from_np(a.dtype), kind="ExternalInput").ap()
           for name, a in arrays.items()}
    out = nc.dram_tensor("out_dram", (B, 1), F32, kind="ExternalOutput").ap()
    build(nc, ins, out)
    r = run_bass_kernel_spmd(nc, [{f"in_{name}_dram": a for name, a in arrays.items()}], core_ids=[0])
    return r.results[0]["out_dram"]
```

```python
from contextlib import ExitStack

import concourse.bass as bass
from concourse import mybir

F32 = mybir.dt.float32
BF16 = mybir.dt.bfloat16
I32 = mybir.dt.int32
ALU = mybir.AluOpType
ACT = mybir.ActivationFunctionType
AX_X = mybir.AxisListType.X

B, F, D, K = 512, 32, 16, 64
P = 128
BLOCKS = B // P
PARTS = 4
PW = P * D // PARTS
HALF = PW // 2
DP = D // PARTS
TILES = F * K // P
TILES0 = 5
NCTX = 16
N1, N2 = 512, 256

PE_TILES = 8
UNITS = PE_TILES // 2
ZSLOTS = 4
LAG = 2
SLOT = [0, 1, 2, 1]
STEPS = [(1, 0), (1, 1), (2, 0), (1, 2), (2, 1), (1, 3), (2, 2), (2, 3)]
POOL_MULS = {(2, 3, 0)}


def tiles_of(layer, g):
    return range(2 * g, min(2 * g + 2, TILES0)) if layer == 0 else range(4 * g, 4 * g + 4)


def groups(layer):
    return 3 if layer == 0 else 4


UNITS_OF = ("wide", "rot", "x0")


class Order:

    def __init__(self):
        self.events, self.waiting = [], []

    def add(self, *events):
        self.events += events

    def product(self, layer, part, g):
        self.add(("mul", layer, part, g))
        self.waiting.append((layer, part, g))
        if len(self.waiting) > LAG:
            self.matmuls()

    def matmuls(self):
        layer, part, g = self.waiting.pop(0)
        self.add(("mm", layer, part, g))
        if g == groups(layer) - 1:
            self.add(("relu", layer, part))
            if part > 0:
                self.add(("sum", layer, part))

    def layer0(self, part, g):
        self.add(("rot", part, g))
        self.product(0, part, g)

    def drain(self):
        while self.waiting:
            self.matmuls()


def turn_order(order, first=False, last=False):
    extra = {}

    def at(begin, end, events):
        for n, event in enumerate(events):
            extra.setdefault(begin + n * (end - begin) // len(events), []).append(event)

    loads = range(PE_TILES // 4, 4)
    at(0, 1, [("load", 1, g) for g in loads])
    at(2, 3, [("load", 2, g) for g in loads])
    at(0, 4, [("wide", 1, u) for u in range(UNITS)])
    at(5, 12, [("wide", 2, u) for u in range(UNITS)])
    at(17, 21, [("wide", 3, u) for u in range(UNITS)])
    for g in loads:
        at(16 + g, 17 + g, [("load", 3, g)])
    if not first:
        at(1, 2, [("fold", 2), ("context", 0)])
        at(3, 4, [("mlp", 1, 0)])
        at(6, 7, [("mlp", 2, 0)])
        at(9, 10, [("mlp", 3, 0)])
    if not last:
        at(0, 1, [("ids", 1)])
        at(0, 16, [("gather", f) for f in range(F)])
        at(17, 18, [("high", 0), ("high", 1)])
        at(18, 19, [("mid", 0), ("mid", 1)])
        at(19, 20, [("turn", 0)])
        at(20, 21, [("x0", 0), ("park", 0), ("turn", 1)])
        at(21, 22, [("x0", 1), ("park", 1), ("turn", 2)])
        at(22, 23, [("x0", 2), ("park", 2)])
        at(23, 24, [("load", 0, g) for g in loads])
        at(23, 24, [("turn", 3)])
        at(25, 26, [("x0", 3), ("park", 3)])
        at(25, 32, [("wide", 0, u) for u in range(UNITS)])
        for n in range(9):
            at(23 + n, 24 + n, [("layer0",) + divmod(n, 3)])
    at(27, 28, [("fold", 1)])

    for n in range(4 * len(STEPS)):
        if n < 3:
            order.layer0(3, n)
        order.product(*STEPS[n // 4], n % 4)
        for event in extra.get(n, []):
            if event[0] == "layer0":
                order.layer0(*event[1:])
            else:
                order.add(event)
    order.drain()
    if last:
        order.add(("fold", 2), ("context", 1), ("mlp", 1, 1), ("mlp", 2, 1), ("mlp", 3, 1))


def first_order():
    order = Order()
    order.add(("ids", 0), *[("gather", f) for f in range(F)])
    order.add(("high", 0), ("high", 1), ("mid", 0), ("mid", 1), ("turn", 0), ("x0", 0), ("park", 0), ("turn", 1))
    order.layer0(0, 0)
    order.add(*[("load", 0, g) for g in range(PE_TILES // 4, 4)])
    order.layer0(0, 1)
    order.add(("x0", 1), ("park", 1))
    order.layer0(0, 2)
    order.layer0(1, 0)
    order.add(("turn", 2), ("wide", 0, 0), ("wide", 0, 1))
    order.layer0(1, 1)
    order.layer0(1, 2)
    order.add(("x0", 2), ("park", 2), ("turn", 3), ("wide", 0, 2))
    for g in range(3):
        order.layer0(2, g)
    order.add(("wide", 0, 3), ("x0", 3), ("park", 3))
    order.drain()
    turn_order(order, first=True)
    return order.events


def order_of(**kind):
    order = Order()
    turn_order(order, **kind)
    return order.events


FIRST, BODY, LAST = first_order(), order_of(), order_of(last=True)


class Phase:

    def __init__(self, events, i):
        self.events, self.i = events, i

    def walk(self):
        for place, event in enumerate(self.events):
            yield Here(self, place), event


class Here:

    def __init__(self, phase, place):
        self.phase, self.place = phase, place

    def had(self, event):
        return self.phase.events is not FIRST or event in self.phase.events[:self.place]

    def back(self, kinds, n):
        own = [e for e in self.phase.events[:self.place] if e[0] in kinds]
        if len(own) >= n:
            return own[-n]
        if self.phase.events is FIRST:
            return None
        return [e for e in BODY if e[0] in kinds][len(own) - n]

    def ring(self, kinds, size):
        before = 0 if self.phase.events is FIRST else sum(e[0] in kinds for e in FIRST)
        return (before - 1 + sum(e[0] in kinds for e in self.phase.events[:self.place + 1])) % size


class Tally:

    def __init__(self, adds):
        self.adds = adds
        self.first, self.turn = (sum(map(adds, e)) for e in (FIRST, BODY))

    def at(self, here, event):
        phase = here.phase
        base = 0 if phase.events is FIRST else (phase.i - 1) * self.turn + self.first
        for place in range(here.place, -1, -1):
            if phase.events[place] == event:
                return base + sum(map(self.adds, phase.events[:place + 1]))
        assert phase.events is not FIRST, event
        rest = []
        for events in (FIRST, BODY):
            place = max(n for n, e in enumerate(events) if e == event)
            rest.append(sum(map(self.adds, events[place + 1:])))
        assert rest[0] == rest[1], event
        return base - rest[0]

    def reaches(self, here, event, steps):
        return here.phase.events is not FIRST or self.at(here, event) > steps


def counts(*kinds, by=1):
    return Tally(lambda e: by * int(e[0] in kinds))


products = counts("mul")
dve_muls = Tally(lambda e: int(e[0] == "mul" and e[1:] not in POOL_MULS))
pool_muls = Tally(lambda e: int(e[0] == "mul" and e[1:] in POOL_MULS))
consumed = counts("mm")
relus = counts("relu", by=4)
sums = counts("sum")
units = counts(*UNITS_OF)
wides = counts("wide")
x0s = counts("x0")
highs = counts("high")
mids = counts("mid")
turns = counts("turn")
gathers = counts("gather", by=16)
idloads = counts("ids", by=16)
folds = Tally(lambda e: {1: 2, 2: 1}[e[1]] if e[0] == "fold" else 0)
contexts = counts("context")
mlps = counts("mlp")
hids = Tally(lambda e: {1: N1 // P, 2: N2 // P, 3: 1}[e[1]] if e[0] == "mlp" else 0)
parks = [Tally(lambda e, p=p: 16 * int(e == ("park", p))) for p in range(PARTS)]
loads_of = {(s, g): Tally(lambda e, s=s, g=g: 32 * int(e[0] == "load" and SLOT[e[1]] == s and e[2] == g))
            for s in range(3) for g in range(4)}


def z_slot(here, event):
    return here.ring(("mm",), ZSLOTS)


def y_bank(layer, part):
    return 2 if layer == 0 else STEPS.index((layer, part)) % 2


assert products.turn % ZSLOTS == 0 and units.turn % 2 == 0


def build(nc, ins, out):
    embeddings = [ins[f"tbl_{f}"] for f in range(F)]
    x0_dram = nc.dram_tensor("x0_parked", (F, P * D), F32, kind="Internal").ap()

    with ExitStack() as ctx:
        def sb(name, shape, dt=F32):
            return ctx.enter_context(nc.sbuf_tensor(name, shape, dt))

        def ps(name, shape):
            return ctx.enter_context(nc.psum_tensor(name, shape, F32))

        def sem(name):
            return ctx.enter_context(nc.semaphore(name))

        idx = sb("idx", [P, F], I32)
        ids_seen = sb("ids_seen", [P, 2], I32)
        gathered = sb("gathered", [P, F * D])
        rest = sb("rest", [P, F * D])
        split = sb("split", [P, D, 3, F], BF16)
        x0_split = sb("x0_split", [P, P * D], BF16)
        x0 = sb("x0", [P, P * D])
        wide = [sb(f"wide{s}", [P, TILES, PW]) for s in range(3)]
        z = sb("z", [P, ZSLOTS, 4, PW])
        xk = sb("xk", [P, PARTS, PW])
        xlast = sb("xlast", [P, 2, PW])
        acc = [sb(f"acc{layer}", [P, PW]) for layer in range(3)]
        pooled01 = sb("pooled01", [P, P])
        pooled2 = sb("pooled2", [P, P])
        context = sb("context", [P, B])
        w0 = sb("w0", [P, TILES0, K])
        w0_mirror = sb("w0_mirror", [P, TILES0, K])
        w12 = sb("w12", [P, 2, TILES, K])
        top1a = sb("top1a", [P, N1])
        top1b = sb("top1b", [P, N1])
        top2 = sb("top2", [P, N1 // P, N2])
        top3 = sb("top3", [P, N2 // P])
        bias1 = sb("bias1", [P, N1 // P])
        bias2 = sb("bias2", [P, N2 // P])
        hid1 = sb("hid1", [P, N1 // P, P])
        hid2 = sb("hid2", [P, N2 // P, P])
        y_row = sb("y_row", [P, B])
        select = sb("select", [P, max(PE_TILES, 1), P], BF16)
        rotate = sb("rotate", [P, TILES0, P], BF16)
        four = sb("four", [P, P], BF16)
        ident = sb("ident", [P, P], BF16)

        ps_wide = ps("ps_wide", [P, 2, 2, PW])
        ps_y = ps("ps_y", [P, 3, 512])
        ps_turn = ps("ps_turn", [P, PW])

        consts_in = sem("consts_in")
        w0_in = sem("w0_in")
        w12_in = sem("w12_in")
        top_in = sem("top_in")
        w0_ready = sem("w0_ready")
        ids_in = sem("ids_in")
        seen_zeroed = sem("seen_zeroed")
        rows_in = sem("rows_in")
        high_ready = sem("high_ready")
        rest_ready = sem("rest_ready")
        mid_ready = sem("mid_ready")
        low_ready = sem("low_ready")
        turned = sem("turned")
        split_ready = sem("split_ready")
        x0_ready = sem("x0_ready")
        parked = [sem(f"parked{p}") for p in range(PARTS)]
        wide_in = [[sem(f"wide_in{s}_{g}") for g in range(4)] for s in range(3)]
        unit_ready = sem("unit_ready")
        wide_ready = sem("wide_ready")
        z_vector = sem("z_vector")
        z_pool = sem("z_pool")
        z_used = sem("z_used")
        xk_ready = sem("xk_ready")
        sum_done = sem("sum_done")
        folded = sem("folded")
        context_ready = sem("context_ready")
        mlp_ready = sem("mlp_ready")
        hid_ready = sem("hid_ready")
        out_done = sem("out_done")

        block = ctx.enter_context(nc.Block())

        def cols(part):
            return slice(part * PW, (part + 1) * PW)

        def wait_product(eng, here, *group):
            if group in POOL_MULS:
                eng.wait_ge(z_pool, pool_muls.at(here, ("mul",) + group))
            else:
                eng.wait_ge(z_vector, dve_muls.at(here, ("mul",) + group))

        def wait_wide_free(eng, here, part, g):
            last = (2, {0: 0, 1: 3, 2: 2, 3: 1}[part], g)
            if here.had(("mul",) + last):
                wait_product(eng, here, *last)

        def wait_wide_ready(eng, here, part, g):
            if 4 * g < PE_TILES:
                eng.wait_ge(wide_ready, wides.at(here, ("wide", part, 2 * g + 1)))
            else:
                eng.wait_ge(wide_in[SLOT[part]][g], loads_of[SLOT[part], g].at(here, ("load", part, g)))

        def by_half(array, h):
            return array[:].rearrange("p (f d) -> p d f", d=D)[:, h * D // 2:(h + 1) * D // 2]

        def third(n, h):
            return split[:, h * D // 2:(h + 1) * D // 2, n]

        def multiply(engine, here, layer, part, g):
            t = tiles_of(layer, g)
            n = len(t)
            one = (xk[:, part, :] if layer else x0[:, cols(part)]).unsqueeze(1).broadcast_to([P, n, PW])
            other = wide[SLOT[part]][:, t[0]:t[0] + n, :] if layer else \
                ps_wide[:, here.ring(UNITS_OF, 2), 0:n]
            return engine.tensor_tensor(z[:, here.ring(("mul",), ZSLOTS), 0:n], one, other, ALU.mult)

        def phases(eng, run):
            run(Phase(FIRST, 0))
            with eng.Fori(1, BLOCKS - 1) as i:
                run(Phase(BODY, i))
            run(Phase(LAST, BLOCKS - 1))

        @block.sync
        def _(sp):
            sp.dma_start(ident[:], ins["ident"]).then_inc(consts_in, 16)
            sp.dma_start(four[0:96], ins["four"]).then_inc(consts_in, 16)
            sp.dma_start(select[0:96], ins["select"]).then_inc(consts_in, 16)
            sp.dma_start(rotate[0:96], ins["rotate"]).then_inc(consts_in, 16)
            sp.dma_start(w0[:], ins["w0_pairs"].rearrange("(t p) k -> p t k", p=P)).then_inc(w0_in, 16)
            sp.dma_start(w0_mirror[:], ins["w0_mirror"].rearrange("(t p) k -> p t k", p=P)).then_inc(w0_in, 16)
            for n in (1, 2):
                sp.dma_start(w12[:, n - 1], ins[f"L0_rec_W{n}"].rearrange("m h k -> (m h) k")
                             .rearrange("(t p) k -> p t k", p=P)).then_inc(w12_in, 16)
            top = ins["W_top1"]
            sp.dma_start(top1a[:], top[0:P, :]).then_inc(top_in, 16)
            sp.dma_start(top1b[0:K + NCTX], top[P:, :]).then_inc(top_in, 16)
            sp.dma_start(top2[:], ins["W_top2"].rearrange("(t p) n -> p t n", p=P)).then_inc(top_in, 16)
            sp.dma_start(top3[:], ins["top3"]).then_inc(top_in, 16)
            sp.dma_start(bias1[:], ins["bias1"]).then_inc(top_in, 16)
            sp.dma_start(bias2[:], ins["bias2"]).then_inc(top_in, 16)
            sp.dma_start(context[K:K + NCTX], ins["context"]).then_inc(top_in, 16)

            def run(phase):
                for here, event in phase.walk():
                    if event[0] == "ids":
                        if here.had(("gather", F - 1)):
                            sp.wait_ge(rows_in, gathers.at(here, ("gather", F - 1)))
                        sp.dma_start(idx[:], ins["ids"][bass.ds((phase.i + event[1]) * P, P), :]).then_inc(ids_in, 16)

            phases(sp, run)
            sp.wait_ge(hid_ready, hids.first + (BLOCKS - 2) * hids.turn + sum(map(hids.adds, LAST)))
            sp.dma_start(out.rearrange("b one -> one b"), y_row[0:1, :]).then_inc(out_done, 16)
            sp.wait_ge(out_done, 16)
            for part in range(PARTS):
                sp.wait_ge(parked[part], 16 * BLOCKS)

        @block.gpsimd
        def _(pool):
            nc.gpsimd.memset(ids_seen[:], 0).then_inc(seen_zeroed, 1)
            pool.wait_ge(seen_zeroed, 1)

            def run(phase):
                for here, event in phase.walk():
                    kind = event[0]
                    if kind == "gather":
                        f = event[1]
                        if f == 0:
                            first = phase.events is FIRST and here.place < phase.events.index(("ids", 1))
                            pool.wait_ge(ids_in, idloads.at(here, ("ids", 0 if first else 1)))
                            nc.gpsimd.tensor_tensor(ids_seen[:, 1:2], ids_seen[:, 0:1], ids_seen[:, 0:1], ALU.add)
                        nc.gpsimd.indirect_dma_start(
                            gathered[:, f * D:(f + 1) * D], None, embeddings[f],
                            bass.IndirectOffsetOnAxis(ap=idx[:, f:f + 1], axis=0)).then_inc(rows_in, 16)
                    elif kind == "high":
                        pool.wait_ge(high_ready, highs.at(here, event))
                        nc.gpsimd.tensor_tensor(by_half(rest, event[1]), by_half(gathered, event[1]),
                                                third(0, event[1]), ALU.subtract).then_inc(rest_ready, 1)
                    elif kind == "mid":
                        pool.wait_ge(mid_ready, mids.at(here, event))
                        nc.gpsimd.tensor_tensor(third(2, event[1]), by_half(rest, event[1]),
                                                third(1, event[1]), ALU.subtract).then_inc(low_ready, 1)
                    elif kind == "sum":
                        _, layer, part = event
                        pool.wait_ge(xk_ready, relus.at(here, ("relu", layer, part)))
                        if part > 1:
                            pool.wait_ge(sum_done, sums.at(here, ("sum", layer, part - 1)))
                        elif layer == 0 and here.had(("fold", 1)):
                            pool.wait_ge(folded, folds.at(here, ("fold", 1)))
                        now, first = (xlast[:, part % 2], xlast[:, 0]) if layer == 2 else (xk[:, part], xk[:, 0])
                        nc.gpsimd.tensor_tensor(acc[layer][:], first if part == 1 else acc[layer][:], now,
                                                ALU.add).then_inc(sum_done, 1)
                    elif kind == "mul" and event[1:] in POOL_MULS:
                        _, layer, part, g = event
                        if products.reaches(here, event, ZSLOTS):
                            pool.wait_ge(z_used, products.at(here, event) - ZSLOTS)
                        pool.wait_ge(xk_ready, relus.at(here, ("relu", layer - 1, part)))
                        wait_wide_ready(pool, here, part, g)
                        multiply(nc.gpsimd, here, *event[1:]).then_inc(z_pool, 1)

            phases(pool, run)

        @block.vector
        def _(dve):
            dve.wait_ge(w0_in, 32)
            nc.vector.tensor_tensor(w0[:], w0[:], w0_mirror[:], ALU.add).then_inc(w0_ready, 1)

            def run(phase):
                for here, event in phase.walk():
                    kind = event[0]
                    if kind == "mul" and event[1:] not in POOL_MULS:
                        _, layer, part, g = event
                        if products.reaches(here, event, ZSLOTS):
                            dve.wait_ge(z_used, products.at(here, event) - ZSLOTS)
                        if layer == 0:
                            dve.wait_ge(x0_ready, x0s.at(here, ("x0", part)))
                            dve.wait_ge(unit_ready, units.at(here, ("rot", part, g)))
                        else:
                            dve.wait_ge(xk_ready, relus.at(here, ("relu", layer - 1, part)))
                            wait_wide_ready(dve, here, part, g)
                        multiply(nc.vector, here, *event[1:]).then_inc(z_vector, 1)
                    elif kind == "fold":
                        dve.wait_ge(sum_done, sums.at(here, ("sum", event[1], PARTS - 1)))
                        for layer in [(), (0, 1), (2,)][event[1]]:
                            rows = slice(K, P) if layer == 1 else slice(0, K)
                            pooled = pooled2 if layer == 2 else pooled01
                            nc.vector.tensor_reduce(pooled[rows], acc[layer][rows].rearrange("p (d b) -> p b d", d=DP),
                                                    AX_X, ALU.add).then_inc(folded, 1)

            phases(dve, run)

        @block.scalar
        def _(act):
            def run(phase):
                for here, event in phase.walk():
                    kind = event[0]
                    if kind == "high":
                        act.wait_ge(rows_in, gathers.at(here, ("gather", F - 1)))
                        if here.had(("turn", 2 * event[1] + 1)):
                            act.wait_ge(turned, turns.at(here, ("turn", 2 * event[1] + 1)))
                        nc.scalar.activation(third(0, event[1]), by_half(gathered, event[1]),
                                             ACT.Copy).then_inc(high_ready, 1)
                    elif kind == "mid":
                        act.wait_ge(rest_ready, highs.at(here, ("high", event[1])))
                        nc.scalar.activation(third(1, event[1]), by_half(rest, event[1]),
                                             ACT.Copy).then_inc(mid_ready, 1)
                    elif kind == "turn":
                        act.wait_ge(turned, turns.at(here, event))
                        nc.scalar.activation(x0_split[0:96, cols(event[1])], ps_turn[0:96],
                                             ACT.Copy).then_inc(split_ready, 1)
                    elif kind == "x0":
                        part = event[1]
                        act.wait_ge(unit_ready, units.at(here, event))
                        if here.had(("park", part)):
                            act.wait_ge(parked[part], parks[part].at(here, ("park", part)))
                        nc.scalar.activation(x0[:, cols(part)], ps_wide[:, here.ring(UNITS_OF, 2), 0],
                                             ACT.Copy).then_inc(x0_ready, 1)
                    elif kind == "park":
                        part = event[1]
                        act.wait_ge(x0_ready, x0s.at(here, ("x0", part)))
                        for g in range(PE_TILES // 4, 4):
                            if here.had(("mul", 1, part, g)):
                                wait_product(act, here, 1, part, g)
                        act.dma_start(x0_dram[:, cols(part)], x0[0:F, cols(part)]).then_inc(parked[part], 16)
                    elif kind == "load":
                        _, part, g = event
                        wait_wide_free(act, here, part, g)
                        act.wait_ge(parked[part], parks[part].at(here, ("park", part)))
                        for half in range(2):
                            src = x0_dram[:, cols(part)].rearrange(
                                "(t two) c -> two t c", two=2)[half:half + 1, 4 * g:4 * g + 4, :]
                            act.dma_start(wide[SLOT[part]][K * half:K * half + K, 4 * g:4 * g + 4, :],
                                          src.broadcast_to([K, 4, PW])).then_inc(wide_in[SLOT[part]][g], 16)
                    elif kind == "wide":
                        _, part, u = event
                        act.wait_ge(unit_ready, units.at(here, event))
                        wait_wide_free(act, here, part, u // 2)
                        nc.scalar.activation(wide[SLOT[part]][:, 2 * u:2 * u + 2, :],
                                             ps_wide[:, here.ring(UNITS_OF, 2)],
                                             ACT.Copy).then_inc(wide_ready, 1)
                    elif kind == "relu":
                        _, layer, part = event
                        act.wait_ge(z_used, consumed.at(here, ("mm", layer, part, groups(layer) - 1)))
                        if layer == 2:
                            summed = ("sum", 2, 3 if part < 2 else 1)
                        else:
                            summed = ("sum", 1 - layer, max(part, 1))
                        if here.had(summed):
                            act.wait_ge(sum_done, sums.at(here, summed))
                        dst = xlast[:, part % 2] if layer == 2 else xk[:, part]
                        for c in range(2):
                            for half in range(2):
                                nc.scalar.activation(dst[K * half:K * half + K, c * HALF:(c + 1) * HALF],
                                                     ps_y[c * K:c * K + K, y_bank(layer, part), 0:HALF],
                                                     ACT.Relu).then_inc(xk_ready, 1)
                    elif kind == "context":
                        act.wait_ge(top_in, 7 * 16)
                        nc.scalar.activation(pooled2[K:K + NCTX],
                                             context[K:K + NCTX, bass.ds((phase.i - 1 + event[1]) * P, P)],
                                             ACT.Copy).then_inc(context_ready, 1)
                    elif kind == "mlp":
                        _, n, own = event
                        act.wait_ge(mlp_ready, mlps.at(here, event))
                        if n == 3:
                            nc.scalar.activation(y_row[0:1, bass.ds((phase.i - 1 + own) * P, P)], ps_turn[0:1, 0:P],
                                                 ACT.Copy).then_inc(hid_ready, 1)
                        hid, bias, chunks = [(hid1, bias1, N1 // P), (hid2, bias2, N2 // P), (None, None, 0)][n - 1]
                        for q in range(chunks):
                            nc.scalar.activation(hid[:, q], ps_turn[:, q * P:(q + 1) * P], ACT.Relu,
                                                 bias=bias[:, q:q + 1]).then_inc(hid_ready, 1)

            phases(act, run)

        @block.tensor
        def _(pe):
            pe.wait_ge(consts_in, 4 * 16)

            def run(phase):
                for here, event in phase.walk():
                    kind = event[0]
                    if kind == "turn":
                        part = event[1]
                        pe.wait_ge(low_ready, mids.at(here, ("mid", part // 2)))
                        if turns.reaches(here, event, 1):
                            pe.wait_ge(split_ready, turns.at(here, event) - 1)
                        for j in range(DP):
                            mm = nc.tensor.matmul(ps_turn[0:96, j * P:(j + 1) * P],
                                                  split[:, part * DP + j].rearrange("p r f -> p (r f)"), ident[:],
                                                  start=True, stop=True)
                        mm.then_inc(turned, 1)
                    elif kind in UNITS_OF:
                        part = event[1]
                        before = here.back(UNITS_OF, 2)
                        if before and before[0] == "wide":
                            pe.wait_ge(wide_ready, wides.at(here, before))
                        elif before and before[0] == "x0":
                            pe.wait_ge(x0_ready, x0s.at(here, before))
                        elif before:
                            wait_product(pe, here, 0, *before[1:])
                        pe.wait_ge(split_ready, turns.at(here, ("turn", part)))
                        buf = here.ring(UNITS_OF, 2)
                        if kind == "wide":
                            tables = [select[0:96, t] for t in range(2 * event[2], 2 * event[2] + 2)]
                        elif kind == "rot":
                            tables = [rotate[0:96, t] for t in tiles_of(0, event[2])]
                        else:
                            tables = [four[0:96]]
                        for n, table in enumerate(tables):
                            mm = nc.tensor.matmul(ps_wide[:, buf, n], table, x0_split[0:96, cols(part)],
                                                  start=True, stop=True)
                        mm.then_inc(unit_ready, 1)
                    elif kind == "mm":
                        _, layer, part, g = event
                        wait_product(pe, here, *event[1:])
                        if g == 0:
                            former = (0, (part - 1) % PARTS) if layer == 0 else STEPS[STEPS.index((layer, part)) - 2]
                            if here.had(("relu",) + former):
                                pe.wait_ge(xk_ready, relus.at(here, ("relu",) + former))
                            if phase.events is FIRST and part == 0:
                                pe.wait_ge(w0_ready, 1)
                                pe.wait_ge(w12_in, 32)
                        slot = z_slot(here, event)
                        total = TILES if layer else TILES0
                        for n, t in enumerate(tiles_of(layer, g)):
                            weights = w12[:, layer - 1, t] if layer else w0[:, t]
                            for c in range(2):
                                mm = nc.tensor.matmul(ps_y[K * c:K * c + K, y_bank(layer, part), 0:HALF], weights,
                                                      z[:, slot, n, c * HALF:(c + 1) * HALF],
                                                      start=t == 0, stop=t == total - 1)
                        mm.then_inc(z_used, 1)
                    elif kind == "mlp" and event[1] == 1:
                        pe.wait_ge(folded, folds.at(here, ("fold", 2)))
                        pe.wait_ge(context_ready, contexts.at(here, ("context", event[2])))
                        for q in range(N1 // P):
                            nc.tensor.matmul(ps_turn[:, q * P:(q + 1) * P], top1a[:, q * P:(q + 1) * P],
                                             pooled01[:], start=True, stop=False)
                            mm = nc.tensor.matmul(ps_turn[:, q * P:(q + 1) * P], top1b[0:K + NCTX, q * P:(q + 1) * P],
                                                  pooled2[0:K + NCTX], start=False, stop=True)
                        mm.then_inc(mlp_ready, 1)
                    elif kind == "mlp" and event[1] == 2:
                        pe.wait_ge(hid_ready, hids.at(here, ("mlp", 1, event[2])))
                        for q in range(N2 // P):
                            for t in range(N1 // P):
                                mm = nc.tensor.matmul(ps_turn[:, q * P:(q + 1) * P], top2[:, t, q * P:(q + 1) * P],
                                                      hid1[:, t], start=t == 0, stop=t == N1 // P - 1)
                        mm.then_inc(mlp_ready, 1)
                    elif kind == "mlp":
                        pe.wait_ge(hid_ready, hids.at(here, ("mlp", 2, event[2])))
                        for t in range(N2 // P):
                            mm = nc.tensor.matmul(ps_turn[0:1, 0:P], top3[:, t:t + 1], hid2[:, t],
                                                  start=t == 0, stop=t == N2 // P - 1)
                        mm.then_inc(mlp_ready, 1)

            phases(pe, run)


def kernel(**inputs):
    import ml_dtypes
    import numpy as np
    from concourse import bacc
    from concourse.bass_utils import run_bass_kernel_spmd

    w = np.asarray(inputs["L0_rec_W0"])
    h = np.arange(F)
    pairs = np.zeros((4 * TILES0, F, K), w.dtype)
    mirror = np.zeros((4 * TILES0, F, K), w.dtype)
    for j in range(F // 2 + 1):
        pairs[j] = w[h, (h + j) % F]
        if 0 < j < F // 2:
            mirror[j] = w[(h + j) % F, h]

    select = np.zeros((3, F, max(PE_TILES, 1), P), np.float32)
    rotate = np.zeros((3, F, TILES0, P), np.float32)
    for t in range(PE_TILES):
        for p in range(P):
            select[:, 2 * t + p // K, t, p] = 1
    for j in range(F // 2 + 1):
        for m in range(F):
            rotate[:, (m + j) % F, j // 4, j % 4 * F + m] = 1

    arrays = {k: np.ascontiguousarray(inputs[k]) for k in
              ["ids"] + [f"tbl_{f}" for f in range(F)]
              + ["W_top1", "W_top2", "L0_rec_W1", "L0_rec_W2"]}
    for name, key in (("bias1", "b_top1"), ("bias2", "b_top2"), ("top3", "W_top3")):
        arrays[name] = np.ascontiguousarray(np.asarray(inputs[key]).reshape(-1, P).T)
    arrays["context"] = np.ascontiguousarray(np.asarray(inputs["dense_ctx"]).T)
    arrays["w0_pairs"] = pairs.reshape(-1, K)
    arrays["w0_mirror"] = mirror.reshape(-1, K)
    arrays["select"] = select.reshape(3 * F, -1, P).astype(ml_dtypes.bfloat16)
    arrays["rotate"] = rotate.reshape(3 * F, -1, P).astype(ml_dtypes.bfloat16)
    arrays["four"] = np.tile(np.eye(F, dtype=np.float32), (3, 4)).astype(ml_dtypes.bfloat16)
    arrays["ident"] = np.eye(P, dtype=np.float32).astype(ml_dtypes.bfloat16)

    nc = bacc.Bacc("TRN2", target_bir_lowering=False, num_devices=1)
    ins = {name: nc.dram_tensor(f"in_{name}_dram", a.shape, mybir.dt.from_np(a.dtype), kind="ExternalInput").ap()
           for name, a in arrays.items()}
    out = nc.dram_tensor("out_dram", (B, 1), F32, kind="ExternalOutput").ap()
    build(nc, ins, out)
    r = run_bass_kernel_spmd(nc, [{f"in_{name}_dram": a for name, a in arrays.items()}], core_ids=[0])
    return r.results[0]["out_dram"]
```
